# Optimizing a Trainium2 kernel written in Bass

```python
import numpy as np
import jax
import jax.numpy as jnp

def _softmax(x, axis=-1):
    return jax.nn.softmax(x, axis=axis)
def _gelu(x):
    return jax.nn.gelu(x, approximate=True)
def _silu(x):
    return jax.nn.silu(x)
def _sigmoid(x):
    return jax.nn.sigmoid(x)
def _layernorm(x, axis=-1, eps=1e-5):
    m = jnp.mean(x, axis=axis, keepdims=True)
    v = jnp.var(x, axis=axis, keepdims=True)
    return (x - m) / jnp.sqrt(v + eps)
def _scatter_add(tgt, idx, src, axis=0):
    return tgt.at[idx].add(src)
def _segment_sum(src, seg, n):
    return jax.ops.segment_sum(src, seg, n)

kernel_name = 'mk_conv_seq_d1_conv_nhwc64_d2a6d4'

def setup_inputs(seed: int = 0):
    np.random.seed(seed)
    _w = jnp.asarray
    def _rec_inputs():
        import jax
        import jax.numpy as jnp
        _gk = jax.random.key(seed)
        x = -7.109e-05 + 0.9999 * jax.random.normal(jax.random.fold_in(_gk, 1), (64, 128, 128, 64), jnp.float32)
        return x
    x = _rec_inputs()
    def _L0_conv_setup():
        import jax, jax.numpy as jnp
        import numpy as np
        B, H, W, C = (64, 128, 128, 64)
        BN_EPS = 0.001
        key = jax.random.key(seed)
        ks = jax.random.split(key, 12)
        u = lambda k, shape: jax.random.uniform(k, shape, jnp.float32, -0.05, 0.05)
        return {'x': jax.random.normal(ks[0], (B, H, W, C), jnp.float32), 'gamma': jnp.ones((C,), jnp.float32), 'beta': jnp.zeros((C,), jnp.float32), 'moving_mean': jax.random.normal(ks[1], (C,), jnp.float32) * 0.1, 'moving_var': jnp.ones((C,), jnp.float32) + jax.random.uniform(ks[2], (C,), jnp.float32) * 0.1, 'Wq': u(ks[3], (C, C)), 'bq': jnp.zeros((C,), jnp.float32), 'Wk': u(ks[4], (C, C)), 'bk': jnp.zeros((C,), jnp.float32), 'Wv': u(ks[5], (C, C)), 'bv': jnp.zeros((C,), jnp.float32), 'Wo': u(ks[6], (C, C)), 'bo': jnp.zeros((C,), jnp.float32)}
    _L0_conv_all = _L0_conv_setup()
    _L0_conv_in = {k: v for k, v in _L0_conv_all.items() if k in ('gamma', 'beta', 'moving_mean', 'moving_var', 'Wq', 'bq', 'Wk', 'bk', 'Wv', 'bv', 'Wo', 'bo', )}
    del _L0_conv_all

    return {
        "x": x,
        "L0_conv_gamma": _L0_conv_in["gamma"],
        "L0_conv_beta": _L0_conv_in["beta"],
        "L0_conv_moving_mean": _L0_conv_in["moving_mean"],
        "L0_conv_moving_var": _L0_conv_in["moving_var"],
        "L0_conv_Wq": _L0_conv_in["Wq"],
        "L0_conv_bq": _L0_conv_in["bq"],
        "L0_conv_Wk": _L0_conv_in["Wk"],
        "L0_conv_bk": _L0_conv_in["bk"],
        "L0_conv_Wv": _L0_conv_in["Wv"],
        "L0_conv_bv": _L0_conv_in["bv"],
        "L0_conv_Wo": _L0_conv_in["Wo"],
        "L0_conv_bo": _L0_conv_in["bo"],
    }

def reference(x, L0_conv_gamma, L0_conv_beta, L0_conv_moving_mean, L0_conv_moving_var, L0_conv_Wq, L0_conv_bq, L0_conv_Wk, L0_conv_bk, L0_conv_Wv, L0_conv_bv, L0_conv_Wo, L0_conv_bo):
    import jax
    import jax.numpy as jnp
    def _L0_conv_ref(x, gamma, beta, moving_mean, moving_var, Wq, bq, Wk, bk, Wv, bv, Wo, bo):
        import jax, jax.numpy as jnp
        import numpy as np
        B, H, W, C = (64, 128, 128, 64)
        BN_EPS = 0.001
        xn = (x - moving_mean) * jax.lax.rsqrt(moving_var + BN_EPS) * gamma + beta
        q = xn @ Wq + bq
        k = xn @ Wk + bk
        v = xn @ Wv + bv
        d = k.shape[-1]
        scores = jnp.einsum('bhid,bhjd->bhij', q, k) * d ** (-0.5)
        attn = jax.nn.softmax(scores, axis=-1)
        out = jnp.einsum('bhij,bhjd->bhid', attn, v)
        out = out @ Wo + bo
        return xn + out

    def _gn(v, G=32, eps=1e-5):
        B_, H_, W_, C_ = v.shape
        g = v.reshape(B_, H_, W_, G, C_ // G)
        m = jnp.mean(g, axis=(1, 2, 4), keepdims=True)
        s = jnp.var(g, axis=(1, 2, 4), keepdims=True)
        return ((g - m) / jnp.sqrt(s + eps)).reshape(v.shape)

    def _ln_c(v, eps=1e-6):
        m = jnp.mean(v, axis=-1, keepdims=True)
        s = jnp.var(v, axis=-1, keepdims=True)
        return (v - m) / jnp.sqrt(s + eps)

    def _ln_t(v, eps=1e-5):
        m = jnp.mean(v, axis=-1, keepdims=True)
        s = jnp.var(v, axis=-1, keepdims=True)
        return (v - m) / jnp.sqrt(s + eps)

    def _to_tokens(v):
        B_, H_, W_, C_ = v.shape
        return v.reshape(B_, H_ * W_, C_)
    def _from_tokens(t, like):
        return t.reshape(like.shape)

    x = _L0_conv_ref(x, L0_conv_gamma, L0_conv_beta, L0_conv_moving_mean, L0_conv_moving_var, L0_conv_Wq, L0_conv_bq, L0_conv_Wk, L0_conv_bk, L0_conv_Wv, L0_conv_bv, L0_conv_Wo, L0_conv_bo)
    return x


_drawn_inputs = setup_inputs


def setup_inputs(seed=0):
    import zlib

    import numpy as np

    out = dict(_drawn_inputs(seed))
    spreads = {'L0_conv_gamma': (1.0, 0.2),
     'L0_conv_beta': (0.0, 0.1),
     'L0_conv_bq': (0.0, 0.8),
     'L0_conv_bk': (0.0, 0.8),
     'L0_conv_bv': (0.0, 0.348),
     'L0_conv_bo': (0.0, 0.1)}
    factors = {'L0_conv_moving_var': 4.037, 'L0_conv_Wq': 8.0, 'L0_conv_Wk': 8.0, 'L0_conv_Wv': 7.619}
    for name, (base, spread) in spreads.items():
        noise = np.random.default_rng([zlib.crc32(name.encode()), seed]).standard_normal(out[name].shape)
        drawn = base * np.exp(spread * noise) if base else spread * noise
        out[name] = jnp.asarray(drawn.astype(out[name].dtype))
    for name, factor in factors.items():
        out[name] = (out[name] * factor).astype(out[name].dtype)
    return out
```

```python
from contextlib import ExitStack

import concourse.bass as bass
from concourse import mybir

F32 = mybir.dt.float32
ALU = mybir.AluOpType
ACT = mybir.ActivationFunctionType
AX_X = mybir.AxisListType.X

BN_EPS = 0.001
GROUP = 4
RING = 4
DMA_INC = 16


def build(nc: bass.Bass, x, gamma, beta, mean, var, wq, bq, wk, bk, wv, bv, wo, bo, out):
    B, H, W, C = x.shape
    PAIRS = GROUP // 2
    N = B * H // GROUP
    VW = C + 2
    SCALE = float(C) ** -0.5
    assert W == 128 and 2 * C == 128 and N % RING == 0 and N >= 3 * RING

    x_groups = x.rearrange("b h w c -> (b h) w c").rearrange("(g s) w c -> g w s c", s=GROUP)
    out_groups = out.rearrange("b h w c -> (b h) w c").rearrange("(g s) w c -> g w s c", s=GROUP)

    with ExitStack() as ctx:
        def sb(name, shape):
            return ctx.enter_context(nc.sbuf_tensor(name, shape, F32))

        def psum(name):
            return ctx.enter_context(nc.psum_tensor(name, [128, 512], F32))

        def sem(name):
            return ctx.enter_context(nc.semaphore(name))

        def sem_ring(name):
            return [sem(f"{name}{i}") for i in range(RING)]

        x_in = sb("x_in", [128, RING, GROUP, C])
        xT = sb("xT", [128, 2, PAIRS, W])
        gT = sb("gT", [128, PAIRS, W])
        v_aug = sb("v_aug", [128, RING, GROUP, VW])
        probs = sb("probs", [128, GROUP, W])
        probsT = sb("probsT", [128, 2, GROUP, W])
        row_max = sb("row_max", [128, RING, GROUP])
        top = sb("top", [128, RING, GROUP])
        neg_top = sb("neg_top", [128, RING, GROUP])
        inv_sum = sb("inv_sum", [128, RING, GROUP])
        attn = sb("attn", [128, RING, GROUP, C])
        resid = sb("resid", [128, RING, GROUP, C])
        y = sb("y", [128, RING, GROUP, C])
        ident = sb("ident", [128, 128])
        w_g = sb("w_g", [128, 2, C])
        w_v = sb("w_v", [128, 2, C + 1])
        g_bias = sb("g_bias", [128, 1])
        t_bias = sb("t_bias", [128, 1])
        a_row = sb("a_row", [128, C])
        r_row = sb("r_row", [128, C])
        w_raw = sb("w_raw", [C, 4, C])
        w_fold = sb("w_fold", [C, 3, C])
        w_foldT = sb("w_foldT", [C, 3, 2, C])
        norm_col = sb("norm_col", [C, 4])
        norm_row = sb("norm_row", [128, 5, C])
        bias_col = sb("bias_col", [C, 3])
        bias_fold = sb("bias_fold", [C, 3])
        bias_wide = sb("bias_wide", [C, 2, 128])
        ab_col = sb("ab_col", [C, 2])
        b_row = sb("b_row", [128, C])
        col_tmp = sb("col_tmp", [C, 3])
        row_tmp = sb("row_tmp", [128, 3, C])

        turns_ps, g_ps, v_ps, probsT_ps = (psum(n) for n in ("turns_ps", "g_ps", "v_ps", "probsT_ps"))
        xT_ps = attn_ps = turns_ps
        score_ps = [ctx.enter_context(nc.psum_tensor(f"score_ps{i}", [128, 2, 512], F32)) for i in range(2)]

        x_loaded = sem_ring("x_loaded")
        y_stored = sem_ring("y_stored")
        xT_made = sem_ring("xT_made")
        g_made = sem_ring("g_made")
        v_made = sem_ring("v_made")
        scores_made = sem_ring("scores_made")
        probsT_made = sem_ring("probsT_made")
        attn_made = sem_ring("attn_made")
        xT_kept = sem_ring("xT_kept")
        max_found = sem_ring("max_found")
        top_found = sem_ring("top_found")
        neg_top_found = sem_ring("neg_top_found")
        sum_inverted = sem_ring("sum_inverted")
        attn_kept = sem_ring("attn_kept")
        g_kept = sem_ring("g_kept")
        v_kept = sem_ring("v_kept")
        probs_found = sem_ring("probs_found")
        probsT_kept = sem_ring("probsT_kept")
        x_scaled = sem_ring("x_scaled")
        resid_found = sem_ring("resid_found")
        y_found = sem_ring("y_found")
        params_loaded = sem("params_loaded")
        pool_const = sem("pool_const")
        dve_setup = sem("dve_setup")
        pe_setup = sem("pe_setup")
        act_setup = sem("act_setup")

        COL_VAR, ROW_VAR, FOLDED, TRANSPOSED, BIASED, WIDE, DVE_READY = 1, 2, 15, 16, 17, 18, 28
        PARAM_DMAS = 4 + 4 + 5 + 3

        def uses(r, n):
            return r + (n // RING + 1)

        def parts(n):
            return n % RING

        block = ctx.enter_context(nc.Block())

        def pipeline(eng, step):
            for t in range(-2, RING):
                step(0, t, True)
            with eng.Fori(1, N // RING - 1) as r:
                for t in range(RING):
                    step(r, t, False)
            for t in range(RING + 2):
                step(N // RING - 1, t, True)

        def exists(r, n, peeled):
            return not peeled or 0 <= RING * r + n < N

        @block.sync
        def _(sp):
            for i, w in enumerate((wq, wk, wv, wo)):
                sp.dma_start(w_raw[:, i, :], w).then_inc(params_loaded, DMA_INC)
            for i, v in enumerate((gamma, beta, mean, var)):
                sp.dma_start(norm_col[:, i:i + 1], v.rearrange("(c o) -> c o", o=1)).then_inc(params_loaded, DMA_INC)
            for i, v in enumerate((gamma, beta, mean, var, bo)):
                sp.dma_start(norm_row[:, i, :], v.rearrange("(o c) -> o c", o=1).broadcast_to([128, C])).then_inc(params_loaded, DMA_INC)
            for i, v in enumerate((bq, bk, bv)):
                sp.dma_start(bias_col[:, i:i + 1], v.rearrange("(c o) -> c o", o=1)).then_inc(params_loaded, DMA_INC)

            def load(r, n, peeled):
                if not exists(r, n, peeled):
                    return
                if not (peeled and RING * r + n < RING):
                    sp.wait_ge(xT_made[parts(n)], uses(r, n - RING))
                    sp.wait_ge(resid_found[parts(n)], uses(r, n - RING))
                sp.dma_start(x_in[:, parts(n), :, :], x_groups[r * RING + n]).then_inc(x_loaded[parts(n)], DMA_INC)

            def store(r, n, peeled):
                if not exists(r, n, peeled):
                    return
                sp.wait_ge(y_found[parts(n)], uses(r, n))
                sp.dma_start(out_groups[r * RING + n], y[:, parts(n), :, :]).then_inc(y_stored[parts(n)], DMA_INC)

            for n in range(RING):
                load(0, n, True)

            def step(r, t, peeled):
                store(r, t - 2, peeled)
                load(r, t + RING + 2, peeled)

            for t in range(-2, RING):
                step(0, t, True)
            with sp.Fori(1, N // RING - 2) as r:
                for t in range(RING):
                    step(r, t, False)
            for t in range(RING):
                step(N // RING - 2, t, True)
            for t in range(RING + 2):
                step(N // RING - 1, t, True)
            for s in y_stored:
                sp.wait_ge(s, DMA_INC * (N // RING))

        @block.gpsimd
        def _(pool):
            nc.gpsimd.memset(ident[:], 0.0).then_inc(pool_const, 1)
            nc.gpsimd.memset(w_g[:], 0.0).then_inc(pool_const, 1)
            nc.gpsimd.memset(w_v[:], 0.0).then_inc(pool_const, 1)
            nc.gpsimd.memset(v_aug[:], 1.0).then_inc(pool_const, 1)
            pool.wait_ge(pool_const, 4)
            nc.gpsimd.affine_select(out=ident[:], in_=ident[:], compare_op=ALU.not_equal, fill=1.0, base=0,
                                    pattern=[[-1, 128]], channel_multiplier=1).then_inc(pool_const, 1)

            a_b = a_row[:, None, :].broadcast_to([128, GROUP, C])
            r_b = r_row[:, None, :].broadcast_to([128, GROUP, C])
            pool.wait_ge(dve_setup, DVE_READY)

            def step(r, t, peeled):
                n = t - 2
                if exists(r, n, peeled):
                    s = parts(n)
                    pool.wait_ge(resid_found[s], uses(r, n))
                    pool.wait_ge(attn_kept[s], uses(r, n))
                    if not (peeled and RING * r + n < RING):
                        pool.wait_ge(y_stored[s], DMA_INC * uses(r, n - RING))
                    nc.gpsimd.tensor_tensor(y[:, s], attn[:, s], resid[:, s], ALU.add).then_inc(y_found[s], 1)
                n = t + 2
                if exists(r, n, peeled):
                    s = parts(n)
                    pool.wait_ge(x_loaded[s], DMA_INC * uses(r, n))
                    if not (peeled and RING * r + n < RING):
                        pool.wait_ge(y_found[s], uses(r, n - RING))
                    nc.gpsimd.tensor_tensor(resid[:, s], x_in[:, s], a_b, ALU.mult).then_inc(x_scaled[s], 1)
                    pool.wait_ge(x_scaled[s], uses(r, n))
                    nc.gpsimd.tensor_tensor(resid[:, s], resid[:, s], r_b, ALU.add).then_inc(resid_found[s], 1)

            pipeline(pool, step)

        @block.scalar
        def _(act):
            act.wait_ge(dve_setup, ROW_VAR)
            nc.scalar.activation(col_tmp[:, 1:2], col_tmp[:, 0:1], ACT.Sqrt).then_inc(act_setup, 1)
            nc.scalar.activation(row_tmp[:, 1, :], row_tmp[:, 0, :], ACT.Sqrt).then_inc(act_setup, 1)

            def step(r, t, peeled):
                n = t - 1
                if exists(r, n, peeled):
                    s = parts(n)
                    act.wait_ge(probsT_made[s], uses(r, n))
                    nc.scalar.activation(probsT[:, n % 2], probsT_ps[:].rearrange("p (s w) -> p s w", s=GROUP), ACT.Copy).then_inc(probsT_kept[s], 1)
                n = t + 1
                if exists(r, n, peeled):
                    s = parts(n)
                    act.wait_ge(g_made[s], uses(r, n))
                    nc.scalar.activation(gT[:], g_ps[:, 0:PAIRS * W], ACT.Identity,
                                         bias=g_bias[:, 0:1]).then_inc(g_kept[s], 1)
                    act.wait_ge(v_made[s], uses(r, n))
                    nc.scalar.activation(v_aug[:, s, :, 0:C + 1],
                                         v_ps[:, 0:GROUP * (C + 1)].rearrange("p (s c) -> p s c", s=GROUP),
                                         ACT.Copy).then_inc(v_kept[s], 1)
                n = t
                if exists(r, n, peeled):
                    s = parts(n)
                    act.wait_ge(neg_top_found[s], uses(r, n))
                    for q in range(GROUP):
                        last = nc.scalar.activation(probs[:, q, :], score_ps[n % 2][:, q % 2, q // 2 * W:(q // 2 + 1) * W], ACT.Exp,
                                                    bias=neg_top[:, s, q:q + 1])
                    last.then_inc(probs_found[s], 1)

            act.wait_ge(dve_setup, DVE_READY)
            pipeline(act, step)

        @block.vector
        def _(dve):
            done = [0]

            def chain(ins):
                done[0] += 1
                ins.then_inc(dve_setup, 1)
                dve.wait_ge(dve_setup, done[0])

            dve.wait_ge(params_loaded, DMA_INC * PARAM_DMAS)
            chain(nc.vector.tensor_scalar(col_tmp[:, 0:1], norm_col[:, 3:4], BN_EPS, None, ALU.add))
            chain(nc.vector.tensor_scalar(row_tmp[:, 0, :], norm_row[:, 3, :], BN_EPS, None, ALU.add))
            assert done[0] == ROW_VAR
            dve.wait_ge(act_setup, 2)
            chain(nc.vector.reciprocal(col_tmp[:, 2:3], col_tmp[:, 1:2]))
            chain(nc.vector.tensor_tensor(ab_col[:, 0:1], col_tmp[:, 2:3], norm_col[:, 0:1], ALU.mult))
            chain(nc.vector.tensor_tensor(ab_col[:, 1:2], ab_col[:, 0:1], norm_col[:, 2:3], ALU.mult))
            chain(nc.vector.tensor_tensor(ab_col[:, 1:2], norm_col[:, 1:2], ab_col[:, 1:2], ALU.subtract))
            chain(nc.vector.reciprocal(row_tmp[:, 2, :], row_tmp[:, 1, :]))
            chain(nc.vector.tensor_tensor(a_row[:], row_tmp[:, 2, :], norm_row[:, 0, :], ALU.mult))
            chain(nc.vector.tensor_tensor(b_row[:], a_row[:], norm_row[:, 2, :], ALU.mult))
            chain(nc.vector.tensor_tensor(b_row[:], norm_row[:, 1, :], b_row[:], ALU.subtract))
            chain(nc.vector.tensor_tensor(b_row[:], b_row[:], norm_row[:, 4, :], ALU.add))
            chain(nc.vector.tensor_scalar(w_fold[:, 0, :], w_raw[:, 0, :], ab_col[:, 0:1], SCALE, ALU.mult, ALU.mult))
            chain(nc.vector.tensor_scalar(w_fold[:, 1, :], w_raw[:, 1, :], ab_col[:, 0:1], None, ALU.mult))
            chain(nc.vector.tensor_scalar(w_fold[:, 2, :], w_raw[:, 2, :], ab_col[:, 0:1], None, ALU.mult))
            dve.wait_ge(pe_setup, 1)
            chain(nc.vector.tensor_tensor(bias_fold[:], xT_ps[0:C, 0:3], bias_col[:], ALU.add))
            assert done[0] == FOLDED
            dve.wait_ge(pe_setup, 2)
            chain(nc.vector.tensor_copy(w_foldT[:], g_ps[0:C, 0:3 * 2 * C].rearrange("p (k h c) -> p k h c", k=3, h=2)))
            assert done[0] == TRANSPOSED
            chain(nc.vector.tensor_scalar(bias_fold[:, 0:1], bias_fold[:, 0:1], SCALE, None, ALU.mult))
            assert done[0] == BIASED
            chain(nc.vector.tensor_copy(bias_wide[:], bias_fold[:, 0:3:2, None].broadcast_to([C, 2, 128])))
            assert done[0] == WIDE
            dve.wait_ge(pe_setup, 3)
            dve.wait_ge(pool_const, 5)
            for h in range(2):
                p = slice(h * C, (h + 1) * C)
                chain(nc.vector.tensor_copy(w_g[p, h, :], v_ps[p, 0:C]))
                chain(nc.vector.tensor_copy(w_v[p, h, 1:C + 1], v_ps[p, C:2 * C]))
                chain(nc.vector.tensor_copy(w_v[p, h, 0:1], v_ps[p, 2 * C + 1:2 * C + 2]))
            chain(nc.vector.tensor_copy(g_bias[:], v_ps[:, 2 * C:2 * C + 1]))
            chain(nc.vector.tensor_copy(t_bias[:], v_ps[:, 2 * C + 2:2 * C + 3]))
            chain(nc.vector.tensor_tensor(r_row[:], v_ps[:, 3 * C:4 * C], b_row[:], ALU.add))
            chain(nc.vector.tensor_copy(col_tmp[:, 0:1], col_tmp[:, 1:2]))
            assert done[0] == DVE_READY, done[0]

            def step(r, t, peeled):
                n = t
                if exists(r, n, peeled):
                    s = parts(n)
                    dve.wait_ge(scores_made[s], uses(r, n))
                    nc.vector.tensor_reduce(row_max[:, s, :], score_ps[n % 2][:, :, 0:PAIRS * W].rearrange("p h (k w) -> p k h w", k=PAIRS),
                                            AX_X, ALU.max).then_inc(max_found[s], 1)
                n = t + 2
                if exists(r, n, peeled):
                    s = parts(n)
                    dve.wait_ge(xT_made[s], uses(r, n))
                    nc.vector.tensor_copy(xT[:, n % 2], xT_ps[:, 0:PAIRS * W].rearrange("p (k w) -> p k w", k=PAIRS)) \
                        .then_inc(xT_kept[s], 1)
                n = t
                if exists(r, n, peeled):
                    s = parts(n)
                    dve.wait_ge(max_found[s], uses(r, n))
                    dve.wait_ge(v_kept[s], uses(r, n))
                    nc.vector.scalar_tensor_tensor(out=top[:, s, :], in0=v_aug[:, s, :, 0], scalar=t_bias[:, 0:1],
                                                   in1=row_max[:, s, :], op0=ALU.add, op1=ALU.add).then_inc(top_found[s], 1)
                    dve.wait_ge(top_found[s], uses(r, n))
                    nc.vector.scalar_tensor_tensor(out=neg_top[:, s, :], in0=v_aug[:, s, :, 0], scalar=t_bias[:, 0:1],
                                                   in1=top[:, s, :], op0=ALU.add, op1=ALU.subtract).then_inc(neg_top_found[s], 1)
                n = t - 2
                if exists(r, n, peeled):
                    s = parts(n)
                    dve.wait_ge(attn_made[s], uses(r, n))
                    rows = attn_ps[:, 0:GROUP * (C + 1)].rearrange("p (s c) -> p s c", s=GROUP)
                    nc.vector.reciprocal(inv_sum[:, s, :], rows[:, :, C]).then_inc(sum_inverted[s], 1)
                    dve.wait_ge(sum_inverted[s], uses(r, n))
                    if not (peeled and RING * r + n < RING):
                        dve.wait_ge(y_found[s], uses(r, n - RING))
                    nc.vector.tensor_tensor(attn[:, s], rows[:, :, 0:C],
                                            inv_sum[:, s, :, None].broadcast_to([128, GROUP, C]),
                                            ALU.mult).then_inc(attn_kept[s], 1)

            pipeline(dve, step)

        @block.tensor
        def _(pe):
            pe.wait_ge(dve_setup, FOLDED - 1)
            for i in range(3):
                last = nc.tensor.matmul(xT_ps[0:C, i:i + 1], w_raw[:, i, :], ab_col[:, 1:2], start=True, stop=True)
            last.then_inc(pe_setup, 1)
            pe.wait_ge(pool_const, 5)
            for i in range(3):
                for h in range(2):
                    last = nc.tensor.transpose(g_ps[0:C, (2 * i + h) * C:(2 * i + h + 1) * C], w_fold[:, i, :],
                                               ident[0:C, 0:C])
            last.then_inc(pe_setup, 1)
            pe.wait_ge(dve_setup, WIDE)
            wqT, wkT, wvT = (w_foldT[:, i].rearrange("p h c -> p (h c)") for i in range(3))
            for o, lhsT, rhs in ((0, wqT, w_foldT[:, 1, 0, :]),
                                 (C, wvT, w_raw[:, 3, :]),
                                 (2 * C, wkT, bias_fold[:, 0:1]),
                                 (2 * C + 1, wqT, bias_fold[:, 1:2]),
                                 (2 * C + 2, bias_wide[:, 0, :], bias_fold[:, 1:2]),
                                 (3 * C, bias_wide[:, 1, :], w_raw[:, 3, :])):
                last = nc.tensor.matmul(v_ps[:, o:o + rhs.shape[1]], lhsT, rhs, start=True, stop=True)
            last.then_inc(pe_setup, 1)
            pe.wait_ge(dve_setup, DVE_READY)

            w_g_all = w_g[:].rearrange("p h c -> p (h c)")
            w_v_all = w_v[:].rearrange("p h c -> p (h c)")

            def step(r, t, peeled):
                n = t
                if exists(r, n, peeled):
                    s = parts(n)
                    pe.wait_ge(g_kept[s], uses(r, n))
                    for q in (0, 1, 2, 3):
                        k, h = q // 2, q % 2
                        p = slice(h * C, (h + 1) * C)
                        last = nc.tensor.matmul(score_ps[n % 2][:, h, k * W:(k + 1) * W], gT[p, k, :], xT[p, n % 2, k, :],
                                                start=True, stop=True)
                    last.then_inc(scores_made[s], 1)
                n = t - 1
                if exists(r, n, peeled):
                    s = parts(n)
                    pe.wait_ge(probs_found[s], uses(r, n))
                    if not (peeled and RING * r + n < 1):
                        pe.wait_ge(probsT_kept[parts(n - 1)], uses(r, n - 1))
                    for q in range(GROUP):
                        last = nc.tensor.transpose(probsT_ps[:, q * W:(q + 1) * W], probs[:, q, :], ident[:])
                    last.then_inc(probsT_made[s], 1)
                n = t + 2
                if exists(r, n, peeled):
                    s = parts(n)
                    pe.wait_ge(x_loaded[s], DMA_INC * uses(r, n))
                    if not (peeled and RING * r + n < RING + 1):
                        pe.wait_ge(attn_kept[parts(n - 5)], uses(r, n - 5))
                    elif RING * r + n > 0:
                        pe.wait_ge(xT_kept[parts(n - 1)], uses(r, n - 1))
                    for k in range(PAIRS):
                        last = nc.tensor.transpose(xT_ps[:, k * W:(k + 1) * W],
                                                   x_in[:, s, 2 * k:2 * k + 2, :].rearrange("p s c -> p (s c)"), ident[:])
                    last.then_inc(xT_made[s], 1)
                n = t + 1
                if exists(r, n, peeled):
                    s = parts(n)
                    pe.wait_ge(xT_kept[s], uses(r, n))
                    nc.tensor.matmul(g_ps[:, 0:PAIRS * W], w_g_all, xT[:, n % 2].rearrange("p k w -> p (k w)"),
                                     start=True, stop=True).then_inc(g_made[s], 1)
                    if not (peeled and RING * r + n < 1):
                        pe.wait_ge(v_kept[parts(n - 1)], uses(r, n - 1))
                    for k in range(PAIRS):
                        last = nc.tensor.matmul(v_ps[:, k * 2 * (C + 1):(k + 1) * 2 * (C + 1)], xT[:, n % 2, k, :], w_v_all,
                                                start=True, stop=True)
                    last.then_inc(v_made[s], 1)
                n = t - 2
                if exists(r, n, peeled):
                    s = parts(n)
                    pe.wait_ge(probsT_kept[s], uses(r, n))
                    if not (peeled and RING * r + n + 4 >= N):
                        pe.wait_ge(xT_kept[s], uses(r, n + 4))
                    else:
                        pe.wait_ge(attn_kept[parts(n - 1)], uses(r, n - 1))
                    for q in range(GROUP):
                        last = nc.tensor.matmul(attn_ps[:, q * (C + 1):(q + 1) * (C + 1)], probsT[:, n % 2, q, :],
                                                v_aug[:, s, q, 1:VW], start=True, stop=True)
                    last.then_inc(attn_made[s], 1)

            pipeline(pe, step)


_PARAMS = ["gamma", "beta", "moving_mean", "moving_var", "Wq", "bq", "Wk", "bk", "Wv", "bv", "Wo", "bo"]


def kernel(**inputs):
    import numpy as np
    import concourse.bacc as bacc
    from concourse.bass_utils import run_bass_kernel_spmd

    nc = bacc.Bacc("TRN2", target_bir_lowering=False, num_devices=1)
    arrays, aps = {}, []
    for name in ["x"] + ["L0_conv_" + p for p in _PARAMS]:
        a = np.ascontiguousarray(inputs[name])
        arrays[f"in_{name}"] = a
        aps.append(nc.dram_tensor(f"in_{name}", a.shape, mybir.dt.from_np(a.dtype), kind="ExternalInput").ap())
    aps.append(nc.dram_tensor("out_0", inputs["x"].shape, F32, kind="ExternalOutput").ap())
    build(nc, *aps)
    r = run_bass_kernel_spmd(nc, [arrays], core_ids=[0])
    return r.results[0]["out_0"]
```

```python
from contextlib import ExitStack

import concourse.bass as bass
from concourse import mybir

F32 = mybir.dt.float32
F32R = mybir.dt.float32r
ALU = mybir.AluOpType
ACT = mybir.ActivationFunctionType
AX_X = mybir.AxisListType.X

BN_EPS = 0.001
GROUP = 4
RING = 4
DMA_INC = 16


def build(nc: bass.Bass, x, gamma, beta, mean, var, wq, bq, wk, bk, wv, bv, wo, bo, out):
    B, H, W, C = x.shape
    PAIRS = GROUP // 2
    N = B * H // GROUP
    VW = C + 2
    SCALE = float(C) ** -0.5
    assert W == 128 and 2 * C == 128 and N % RING == 0 and N >= 3 * RING

    x_groups = x.rearrange("b h w c -> (b h) w c").rearrange("(g s) w c -> g w s c", s=GROUP)
    out_groups = out.rearrange("b h w c -> (b h) w c").rearrange("(g s) w c -> g w s c", s=GROUP)

    with ExitStack() as ctx:
        def sb(name, shape, dtype=F32):
            return ctx.enter_context(nc.sbuf_tensor(name, shape, dtype))

        def psum(name):
            return ctx.enter_context(nc.psum_tensor(name, [128, 512], F32))

        def sem(name):
            return ctx.enter_context(nc.semaphore(name))

        def sem_ring(name):
            return [sem(f"{name}{i}") for i in range(RING)]

        x_in = sb("x_in", [128, RING, GROUP, C])
        xT = sb("xT", [128, 2, PAIRS, W])
        xT_high = sb("xT_high", [128, 2, PAIRS, W], F32R)
        xT_low = sb("xT_low", [128, 2, PAIRS, W], F32R)
        gT = sb("gT", [128, PAIRS, W])
        v_aug = sb("v_aug", [128, RING, GROUP, VW])
        probs = sb("probs", [128, GROUP, W])
        probsT = sb("probsT", [128, 2, GROUP, W])
        row_max = sb("row_max", [128, RING, GROUP])
        top = sb("top", [128, RING, GROUP])
        neg_top = sb("neg_top", [128, RING, GROUP])
        inv_sum = sb("inv_sum", [128, RING, GROUP])
        attn = sb("attn", [128, RING, GROUP, C])
        resid = sb("resid", [128, RING, GROUP, C])
        y = sb("y", [128, RING, GROUP, C])
        ident = sb("ident", [128, 128])
        w_g = sb("w_g", [128, 2, C])
        w_g_high = sb("w_g_high", [128, 2, C], F32R)
        w_g_low = sb("w_g_low", [128, 2, C], F32R)
        w_v = sb("w_v", [128, 2, C + 1])
        g_bias = sb("g_bias", [128, 1])
        t_bias = sb("t_bias", [128, 1])
        a_row = sb("a_row", [128, C])
        r_row = sb("r_row", [128, C])
        w_raw = sb("w_raw", [C, 4, C])
        w_fold = sb("w_fold", [C, 3, C])
        w_foldT = sb("w_foldT", [C, 3, 2, C])
        norm_col = sb("norm_col", [C, 4])
        norm_row = sb("norm_row", [128, 5, C])
        bias_col = sb("bias_col", [C, 3])
        bias_fold = sb("bias_fold", [C, 3])
        bias_wide = sb("bias_wide", [C, 2, 128])
        ab_col = sb("ab_col", [C, 2])
        b_row = sb("b_row", [128, C])
        col_tmp = sb("col_tmp", [C, 3])
        row_tmp = sb("row_tmp", [128, 3, C])

        g_ps, v_ps, probsT_ps, attn_ps = (psum(n) for n in ("g_ps", "v_ps", "probsT_ps", "attn_ps"))
        score_ps = [ctx.enter_context(nc.psum_tensor(f"score_ps{i}", [128, 2, 512], F32)) for i in range(2)]

        def xT_ps(n):
            return score_ps[(n - 1) % 2][:, 0, 0:PAIRS * W]

        x_loaded = sem_ring("x_loaded")
        y_stored = sem_ring("y_stored")
        xT_made = sem_ring("xT_made")
        g_made = sem_ring("g_made")
        v_made = sem_ring("v_made")
        scores_made = sem_ring("scores_made")
        probsT_made = sem_ring("probsT_made")
        attn_made = sem_ring("attn_made")
        xT_kept = sem_ring("xT_kept")
        xT_rounded = sem_ring("xT_rounded")
        xT_split = sem_ring("xT_split")
        max_found = sem_ring("max_found")
        top_found = sem_ring("top_found")
        neg_top_found = sem_ring("neg_top_found")
        sum_inverted = sem_ring("sum_inverted")
        attn_kept = sem_ring("attn_kept")
        g_kept = sem_ring("g_kept")
        v_kept = sem_ring("v_kept")
        probs_found = sem_ring("probs_found")
        probsT_kept = sem_ring("probsT_kept")
        x_scaled = sem_ring("x_scaled")
        resid_found = sem_ring("resid_found")
        y_found = sem_ring("y_found")
        params_loaded = sem("params_loaded")
        pool_const = sem("pool_const")
        dve_setup = sem("dve_setup")
        pe_setup = sem("pe_setup")
        act_setup = sem("act_setup")

        COL_VAR, ROW_VAR, FOLDED, TRANSPOSED, BIASED, WIDE, DVE_READY = 1, 2, 23, 24, 25, 26, 37
        PARAM_DMAS = 4 + 4 + 5 + 3

        class Turn:

            def __init__(self, eng, r, dma):
                self.r = r
                self.uses = {k: eng.snap(r + k) if k else r for k in range(-1, 3)}
                self.dma = {k: eng.snap((r + k) * DMA_INC) for k in range(-1, 3)} if dma else {}

        def uses(r, n):
            k = n // RING + 1
            return r + k if isinstance(r, int) else r.uses[k]

        def dma_uses(r, n):
            k = n // RING + 1
            return DMA_INC * (r + k) if isinstance(r, int) else r.dma[k]

        def group(r, n):
            return (r if isinstance(r, int) else r.r) * RING + n

        def parts(n):
            return n % RING

        block = ctx.enter_context(nc.Block())

        def pipeline(eng, step, dma=False):
            for t in range(-2, 2 * RING):
                step(0, t, True)
            with eng.Fori(2, N // RING - 1) as r:
                turn = Turn(eng, r, dma)
                for t in range(RING):
                    step(turn, t, False)
            for t in range(RING + 2):
                step(N // RING - 1, t, True)

        def exists(r, n, peeled):
            return not peeled or 0 <= group(r, n) < N

        @block.sync
        def _(sp):
            for i, w in enumerate((wq, wk, wv, wo)):
                sp.dma_start(w_raw[:, i, :], w).then_inc(params_loaded, DMA_INC)
            for i, v in enumerate((gamma, beta, mean, var)):
                sp.dma_start(norm_col[:, i:i + 1], v.rearrange("(c o) -> c o", o=1)).then_inc(params_loaded, DMA_INC)
            for i, v in enumerate((gamma, beta, mean, var, bo)):
                sp.dma_start(norm_row[:, i, :], v.rearrange("(o c) -> o c", o=1).broadcast_to([128, C])).then_inc(params_loaded, DMA_INC)
            for i, v in enumerate((bq, bk, bv)):
                sp.dma_start(bias_col[:, i:i + 1], v.rearrange("(c o) -> c o", o=1)).then_inc(params_loaded, DMA_INC)

            def load(r, n, peeled):
                if not exists(r, n, peeled):
                    return
                if not (peeled and group(r, n) < RING):
                    sp.wait_ge(xT_made[parts(n)], uses(r, n - RING))
                    sp.wait_ge(resid_found[parts(n)], uses(r, n - RING))
                sp.dma_start(x_in[:, parts(n), :, :], x_groups[group(r, n)]).then_inc(x_loaded[parts(n)], DMA_INC)

            def store(r, n, peeled):
                if not exists(r, n, peeled):
                    return
                sp.wait_ge(y_found[parts(n)], uses(r, n))
                sp.dma_start(out_groups[group(r, n)], y[:, parts(n), :, :]).then_inc(y_stored[parts(n)], DMA_INC)

            for n in range(RING):
                load(0, n, True)

            def step(r, t, peeled):
                store(r, t - 2, peeled)
                load(r, t + RING + 2, peeled)

            for t in range(-2, 2 * RING):
                step(0, t, True)
            with sp.Fori(2, N // RING - 2) as r:
                turn = Turn(sp, r, False)
                for t in range(RING):
                    step(turn, t, False)
            for t in range(RING):
                step(N // RING - 2, t, True)
            for t in range(RING + 2):
                step(N // RING - 1, t, True)
            for s in y_stored:
                sp.wait_ge(s, DMA_INC * (N // RING))

        @block.gpsimd
        def _(pool):
            nc.gpsimd.memset(ident[:], 0.0).then_inc(pool_const, 1)
            nc.gpsimd.memset(w_g[:], 0.0).then_inc(pool_const, 1)
            nc.gpsimd.memset(w_v[:], 0.0).then_inc(pool_const, 1)
            nc.gpsimd.memset(v_aug[:], 1.0).then_inc(pool_const, 1)
            pool.wait_ge(pool_const, 4)
            nc.gpsimd.affine_select(out=ident[:], in_=ident[:], compare_op=ALU.not_equal, fill=1.0, base=0,
                                    pattern=[[-1, 128]], channel_multiplier=1).then_inc(pool_const, 1)

            a_b = a_row[:, None, :].broadcast_to([128, GROUP, C])
            r_b = r_row[:, None, :].broadcast_to([128, GROUP, C])
            pool.wait_ge(dve_setup, DVE_READY)

            def step(r, t, peeled):
                n = t + 2
                if exists(r, n, peeled):
                    s = parts(n)
                    pool.wait_ge(xT_rounded[s], uses(r, n))
                    nc.gpsimd.tensor_tensor(xT_low[:, n % 2], xT[:, n % 2], xT_high[:, n % 2],
                                            ALU.subtract).then_inc(xT_split[s], 1)
                n = t - 2
                if exists(r, n, peeled):
                    s = parts(n)
                    pool.wait_ge(resid_found[s], uses(r, n))
                    pool.wait_ge(attn_kept[s], uses(r, n))
                    if not (peeled and group(r, n) < RING):
                        pool.wait_ge(y_stored[s], dma_uses(r, n - RING))
                    nc.gpsimd.tensor_tensor(y[:, s], attn[:, s], resid[:, s], ALU.add).then_inc(y_found[s], 1)
                n = t + 2
                if exists(r, n, peeled):
                    s = parts(n)
                    pool.wait_ge(x_loaded[s], dma_uses(r, n))
                    if not (peeled and group(r, n) < RING):
                        pool.wait_ge(y_found[s], uses(r, n - RING))
                    nc.gpsimd.tensor_tensor(resid[:, s], x_in[:, s], a_b, ALU.mult).then_inc(x_scaled[s], 1)
                    pool.wait_ge(x_scaled[s], uses(r, n))
                    nc.gpsimd.tensor_tensor(resid[:, s], resid[:, s], r_b, ALU.add).then_inc(resid_found[s], 1)

            pipeline(pool, step, dma=True)

        @block.scalar
        def _(act):
            act.wait_ge(dve_setup, ROW_VAR)
            nc.scalar.activation(col_tmp[:, 1:2], col_tmp[:, 0:1], ACT.Sqrt).then_inc(act_setup, 1)
            nc.scalar.activation(row_tmp[:, 1, :], row_tmp[:, 0, :], ACT.Sqrt).then_inc(act_setup, 1)

            def step(r, t, peeled):
                n = t - 1
                if exists(r, n, peeled):
                    s = parts(n)
                    act.wait_ge(probsT_made[s], uses(r, n))
                    nc.scalar.activation(probsT[:, n % 2], probsT_ps[:].rearrange("p (s w) -> p s w", s=GROUP), ACT.Copy).then_inc(probsT_kept[s], 1)
                n = t + 1
                if exists(r, n, peeled):
                    s = parts(n)
                    act.wait_ge(g_made[s], uses(r, n))
                    nc.scalar.activation(gT[:], g_ps[:, 0:PAIRS * W], ACT.Identity,
                                         bias=g_bias[:, 0:1]).then_inc(g_kept[s], 1)
                    act.wait_ge(v_made[s], uses(r, n))
                    nc.scalar.activation(v_aug[:, s, :, 0:C + 1],
                                         v_ps[:, 0:GROUP * (C + 1)].rearrange("p (s c) -> p s c", s=GROUP),
                                         ACT.Copy).then_inc(v_kept[s], 1)
                n = t
                if exists(r, n, peeled):
                    s = parts(n)
                    act.wait_ge(neg_top_found[s], uses(r, n))
                    for q in range(GROUP):
                        last = nc.scalar.activation(probs[:, q, :], score_ps[n % 2][:, q % 2, q // 2 * W:(q // 2 + 1) * W], ACT.Exp,
                                                    bias=neg_top[:, s, q:q + 1])
                    last.then_inc(probs_found[s], 1)

            act.wait_ge(dve_setup, DVE_READY)
            pipeline(act, step)

        @block.vector
        def _(dve):
            done = [0]

            def chain(ins):
                done[0] += 1
                ins.then_inc(dve_setup, 1)
                dve.wait_ge(dve_setup, done[0])

            dve.wait_ge(params_loaded, DMA_INC * PARAM_DMAS)
            chain(nc.vector.tensor_scalar(col_tmp[:, 0:1], norm_col[:, 3:4], BN_EPS, None, ALU.add))
            chain(nc.vector.tensor_scalar(row_tmp[:, 0, :], norm_row[:, 3, :], BN_EPS, None, ALU.add))
            assert done[0] == ROW_VAR
            dve.wait_ge(act_setup, 2)

            def refine(root, v, tmp):
                chain(nc.vector.tensor_tensor(tmp, root, root, ALU.mult))
                chain(nc.vector.tensor_tensor(tmp, tmp, v, ALU.mult))
                chain(nc.vector.tensor_scalar(tmp, tmp, -0.5, 1.5, ALU.mult, ALU.add))
                chain(nc.vector.tensor_tensor(root, root, tmp, ALU.mult))

            chain(nc.vector.reciprocal(col_tmp[:, 2:3], col_tmp[:, 1:2]))
            refine(col_tmp[:, 2:3], col_tmp[:, 0:1], col_tmp[:, 1:2])
            chain(nc.vector.tensor_tensor(ab_col[:, 0:1], col_tmp[:, 2:3], norm_col[:, 0:1], ALU.mult))
            chain(nc.vector.tensor_tensor(ab_col[:, 1:2], ab_col[:, 0:1], norm_col[:, 2:3], ALU.mult))
            chain(nc.vector.tensor_tensor(ab_col[:, 1:2], norm_col[:, 1:2], ab_col[:, 1:2], ALU.subtract))
            chain(nc.vector.reciprocal(row_tmp[:, 2, :], row_tmp[:, 1, :]))
            refine(row_tmp[:, 2, :], row_tmp[:, 0, :], row_tmp[:, 1, :])
            chain(nc.vector.tensor_tensor(a_row[:], row_tmp[:, 2, :], norm_row[:, 0, :], ALU.mult))
            chain(nc.vector.tensor_tensor(b_row[:], a_row[:], norm_row[:, 2, :], ALU.mult))
            chain(nc.vector.tensor_tensor(b_row[:], norm_row[:, 1, :], b_row[:], ALU.subtract))
            chain(nc.vector.tensor_tensor(b_row[:], b_row[:], norm_row[:, 4, :], ALU.add))
            chain(nc.vector.tensor_scalar(w_fold[:, 0, :], w_raw[:, 0, :], ab_col[:, 0:1], SCALE, ALU.mult, ALU.mult))
            chain(nc.vector.tensor_scalar(w_fold[:, 1, :], w_raw[:, 1, :], ab_col[:, 0:1], None, ALU.mult))
            chain(nc.vector.tensor_scalar(w_fold[:, 2, :], w_raw[:, 2, :], ab_col[:, 0:1], None, ALU.mult))
            dve.wait_ge(pe_setup, 1)
            chain(nc.vector.tensor_tensor(bias_fold[:], attn_ps[0:C, 0:3], bias_col[:], ALU.add))
            assert done[0] == FOLDED
            dve.wait_ge(pe_setup, 2)
            chain(nc.vector.tensor_copy(w_foldT[:], g_ps[0:C, 0:3 * 2 * C].rearrange("p (k h c) -> p k h c", k=3, h=2)))
            assert done[0] == TRANSPOSED
            chain(nc.vector.tensor_scalar(bias_fold[:, 0:1], bias_fold[:, 0:1], SCALE, None, ALU.mult))
            assert done[0] == BIASED
            chain(nc.vector.tensor_copy(bias_wide[:], bias_fold[:, 0:3:2, None].broadcast_to([C, 2, 128])))
            assert done[0] == WIDE
            dve.wait_ge(pe_setup, 3)
            dve.wait_ge(pool_const, 5)
            for h in range(2):
                p = slice(h * C, (h + 1) * C)
                chain(nc.vector.tensor_copy(w_g[p, h, :], v_ps[p, 0:C]))
                chain(nc.vector.tensor_copy(w_v[p, h, 1:C + 1], v_ps[p, C:2 * C]))
                chain(nc.vector.tensor_copy(w_v[p, h, 0:1], v_ps[p, 2 * C + 1:2 * C + 2]))
            chain(nc.vector.tensor_copy(w_g_high[:], w_g[:]))
            chain(nc.vector.tensor_tensor(w_g_low[:], w_g[:], w_g_high[:], ALU.subtract))
            chain(nc.vector.tensor_copy(g_bias[:], v_ps[:, 2 * C:2 * C + 1]))
            chain(nc.vector.tensor_copy(t_bias[:], v_ps[:, 2 * C + 2:2 * C + 3]))
            chain(nc.vector.tensor_tensor(r_row[:], v_ps[:, 3 * C:4 * C], b_row[:], ALU.add))
            assert done[0] == DVE_READY, done[0]

            def step(r, t, peeled):
                n = t
                if exists(r, n, peeled):
                    s = parts(n)
                    dve.wait_ge(scores_made[s], uses(r, n))
                    nc.vector.tensor_reduce(row_max[:, s, :], score_ps[n % 2][:, :, 0:PAIRS * W].rearrange("p h (k w) -> p k h w", k=PAIRS),
                                            AX_X, ALU.max).then_inc(max_found[s], 1)
                n = t + 2
                if exists(r, n, peeled):
                    s = parts(n)
                    dve.wait_ge(xT_made[s], uses(r, n))
                    nc.vector.tensor_copy(xT[:, n % 2], xT_ps(n).rearrange("p (k w) -> p k w", k=PAIRS)) \
                        .then_inc(xT_kept[s], 1)
                n = t
                if exists(r, n, peeled):
                    s = parts(n)
                    dve.wait_ge(max_found[s], uses(r, n))
                    dve.wait_ge(v_kept[s], uses(r, n))
                    nc.vector.scalar_tensor_tensor(out=top[:, s, :], in0=v_aug[:, s, :, 0], scalar=t_bias[:, 0:1],
                                                   in1=row_max[:, s, :], op0=ALU.add, op1=ALU.add).then_inc(top_found[s], 1)
                    dve.wait_ge(top_found[s], uses(r, n))
                    nc.vector.scalar_tensor_tensor(out=neg_top[:, s, :], in0=v_aug[:, s, :, 0], scalar=t_bias[:, 0:1],
                                                   in1=top[:, s, :], op0=ALU.add, op1=ALU.subtract).then_inc(neg_top_found[s], 1)
                n = t + 2
                if exists(r, n, peeled):
                    s = parts(n)
                    dve.wait_ge(xT_kept[s], uses(r, n))
                    nc.vector.tensor_copy(xT_high[:, n % 2], xT[:, n % 2]).then_inc(xT_rounded[s], 1)
                n = t - 2
                if exists(r, n, peeled):
                    s = parts(n)
                    dve.wait_ge(attn_made[s], uses(r, n))
                    rows = attn_ps[:, 0:GROUP * (C + 1)].rearrange("p (s c) -> p s c", s=GROUP)
                    nc.vector.reciprocal(inv_sum[:, s, :], rows[:, :, C]).then_inc(sum_inverted[s], 1)
                    dve.wait_ge(sum_inverted[s], uses(r, n))
                    if not (peeled and group(r, n) < RING):
                        dve.wait_ge(y_found[s], uses(r, n - RING))
                    nc.vector.tensor_tensor(attn[:, s], rows[:, :, 0:C],
                                            inv_sum[:, s, :, None].broadcast_to([128, GROUP, C]),
                                            ALU.mult).then_inc(attn_kept[s], 1)

            pipeline(dve, step)

        @block.tensor
        def _(pe):
            pe.wait_ge(dve_setup, FOLDED - 1)
            for i in range(3):
                last = nc.tensor.matmul(attn_ps[0:C, i:i + 1], w_raw[:, i, :], ab_col[:, 1:2], start=True, stop=True)
            last.then_inc(pe_setup, 1)
            pe.wait_ge(pool_const, 5)
            for i in range(3):
                for h in range(2):
                    last = nc.tensor.transpose(g_ps[0:C, (2 * i + h) * C:(2 * i + h + 1) * C], w_fold[:, i, :],
                                               ident[0:C, 0:C])
            last.then_inc(pe_setup, 1)
            pe.wait_ge(dve_setup, WIDE)
            wqT, wkT, wvT = (w_foldT[:, i].rearrange("p h c -> p (h c)") for i in range(3))
            for o, lhsT, rhs in ((0, wqT, w_foldT[:, 1, 0, :]),
                                 (C, wvT, w_raw[:, 3, :]),
                                 (2 * C, wkT, bias_fold[:, 0:1]),
                                 (2 * C + 1, wqT, bias_fold[:, 1:2]),
                                 (2 * C + 2, bias_wide[:, 0, :], bias_fold[:, 1:2]),
                                 (3 * C, bias_wide[:, 1, :], w_raw[:, 3, :])):
                last = nc.tensor.matmul(v_ps[:, o:o + rhs.shape[1]], lhsT, rhs, start=True, stop=True)
            last.then_inc(pe_setup, 1)
            pe.wait_ge(dve_setup, DVE_READY)

            w_g_high_all = w_g_high[:].rearrange("p h c -> p (h c)")
            w_g_low_all = w_g_low[:].rearrange("p h c -> p (h c)")
            w_v_all = w_v[:].rearrange("p h c -> p (h c)")

            def step(r, t, peeled):
                n = t
                if exists(r, n, peeled):
                    s = parts(n)
                    pe.wait_ge(g_kept[s], uses(r, n))
                    if not (peeled and group(r, n) > N - 2):
                        pe.wait_ge(xT_kept[parts(n + 1)], uses(r, n + 1))
                    for q in (0, 1, 2, 3):
                        k, h = q // 2, q % 2
                        p = slice(h * C, (h + 1) * C)
                        last = nc.tensor.matmul(score_ps[n % 2][:, h, k * W:(k + 1) * W], gT[p, k, :], xT[p, n % 2, k, :],
                                                start=True, stop=True)
                    last.then_inc(scores_made[s], 1)
                n = t - 1
                if exists(r, n, peeled):
                    s = parts(n)
                    pe.wait_ge(probs_found[s], uses(r, n))
                    if not (peeled and group(r, n) < 1):
                        pe.wait_ge(probsT_kept[parts(n - 1)], uses(r, n - 1))
                    for q in range(GROUP):
                        last = nc.tensor.transpose(probsT_ps[:, q * W:(q + 1) * W], probs[:, q, :], ident[:])
                    last.then_inc(probsT_made[s], 1)
                n = t + 2
                if exists(r, n, peeled):
                    s = parts(n)
                    pe.wait_ge(x_loaded[s], dma_uses(r, n))
                    if not (peeled and group(r, n) < 3):
                        pe.wait_ge(probs_found[parts(n - 3)], uses(r, n - 3))
                    elif group(r, n) == 2:
                        pe.wait_ge(xT_kept[parts(n - 2)], uses(r, n - 2))
                    for k in range(PAIRS):
                        last = nc.tensor.transpose(xT_ps(n)[:, k * W:(k + 1) * W],
                                                   x_in[:, s, 2 * k:2 * k + 2, :].rearrange("p s c -> p (s c)"), ident[:])
                    last.then_inc(xT_made[s], 1)
                n = t + 1
                if exists(r, n, peeled):
                    s = parts(n)
                    pe.wait_ge(xT_kept[s], uses(r, n))
                    pe.wait_ge(xT_split[s], uses(r, n))
                    g_parts = ((w_g_low_all, xT_high), (w_g_high_all, xT_low), (w_g_high_all, xT_high))
                    for i, (w_part, x_part) in enumerate(g_parts):
                        last = nc.tensor.matmul(g_ps[:, 0:PAIRS * W], w_part, x_part[:, n % 2].rearrange("p k w -> p (k w)"),
                                                start=(i == 0), stop=(i == len(g_parts) - 1))
                    last.then_inc(g_made[s], 1)
                    if not (peeled and group(r, n) < 1):
                        pe.wait_ge(v_kept[parts(n - 1)], uses(r, n - 1))
                    for k in range(PAIRS):
                        last = nc.tensor.matmul(v_ps[:, k * 2 * (C + 1):(k + 1) * 2 * (C + 1)], xT[:, n % 2, k, :], w_v_all,
                                                start=True, stop=True)
                    last.then_inc(v_made[s], 1)
                n = t - 2
                if exists(r, n, peeled):
                    s = parts(n)
                    pe.wait_ge(probsT_kept[s], uses(r, n))
                    if not (peeled and group(r, n) < 1):
                        pe.wait_ge(attn_kept[parts(n - 1)], uses(r, n - 1))
                    for q in range(GROUP):
                        last = nc.tensor.matmul(attn_ps[:, q * (C + 1):(q + 1) * (C + 1)], probsT[:, n % 2, q, :],
                                                v_aug[:, s, q, 1:VW], start=True, stop=True)
                    last.then_inc(attn_made[s], 1)

            pipeline(pe, step, dma=True)


_PARAMS = ["gamma", "beta", "moving_mean", "moving_var", "Wq", "bq", "Wk", "bk", "Wv", "bv", "Wo", "bo"]


def kernel(**inputs):
    import numpy as np
    import concourse.bacc as bacc
    from concourse.bass_utils import run_bass_kernel_spmd

    nc = bacc.Bacc("TRN2", target_bir_lowering=False, num_devices=1)
    arrays, aps = {}, []
    for name in ["x"] + ["L0_conv_" + p for p in _PARAMS]:
        a = np.ascontiguousarray(inputs[name])
        arrays[f"in_{name}"] = a
        aps.append(nc.dram_tensor(f"in_{name}", a.shape, mybir.dt.from_np(a.dtype), kind="ExternalInput").ap())
    aps.append(nc.dram_tensor("out_0", inputs["x"].shape, F32, kind="ExternalOutput").ap())
    build(nc, *aps)
    r = run_bass_kernel_spmd(nc, [arrays], core_ids=[0])
    return r.results[0]["out_0"]
```

```python
from contextlib import ExitStack

import concourse.bass as bass
from concourse import mybir

F32 = mybir.dt.float32
F32R = mybir.dt.float32r
ALU = mybir.AluOpType
ACT = mybir.ActivationFunctionType
AX_X = mybir.AxisListType.X

BN_EPS = 0.001
GROUP = 4
RING = 4
DMA_INC = 16


def build(nc: bass.Bass, x, gamma, beta, mean, var, wq, bq, wk, bk, wv, bv, wo, bo, out):
    B, H, W, C = x.shape
    PAIRS = GROUP // 2
    N = B * H // GROUP
    VW = C + 2
    SCALE = float(C) ** -0.5
    assert W == 128 and 2 * C == 128 and N % RING == 0 and N >= 3 * RING

    x_groups = x.rearrange("b h w c -> (b h) w c").rearrange("(g s) w c -> g w s c", s=GROUP)
    out_groups = out.rearrange("b h w c -> (b h) w c").rearrange("(g s) w c -> g w s c", s=GROUP)

    with ExitStack() as ctx:
        def sb(name, shape, dtype=F32):
            return ctx.enter_context(nc.sbuf_tensor(name, shape, dtype))

        def psum(name):
            return ctx.enter_context(nc.psum_tensor(name, [128, 512], F32))

        def sem(name):
            return ctx.enter_context(nc.semaphore(name))

        def sem_ring(name):
            return [sem(f"{name}{i}") for i in range(RING)]

        x_in = sb("x_in", [128, RING, GROUP, C])
        xT = sb("xT", [128, 2, PAIRS, W])
        xT_high = sb("xT_high", [128, 2, PAIRS, W], F32R)
        xT_low = sb("xT_low", [128, 2, PAIRS, W], F32R)
        x_diag = sb("x_diag", [128, 2, 2, PAIRS, 2, W], F32R)
        g_high = sb("g_high", [128, PAIRS, W], F32R)
        g_low = sb("g_low", [128, PAIRS, W], F32R)
        v_aug = sb("v_aug", [128, RING, GROUP, VW])
        probs = sb("probs", [128, GROUP, W])
        probsT = sb("probsT", [128, 2, GROUP, W])
        row_max = sb("row_max", [128, RING, GROUP])
        top = sb("top", [128, RING, GROUP])
        neg_top = sb("neg_top", [128, RING, GROUP])
        inv_sum = sb("inv_sum", [128, RING, GROUP])
        x_scaled_rows = sb("x_scaled_rows", [128, RING, GROUP, C])
        attn = sb("attn", [128, GROUP, C])
        y = sb("y", [128, RING, GROUP, C])
        ident = sb("ident", [128, 128])
        w_g = sb("w_g", [128, 2, C])
        w_g_high = sb("w_g_high", [128, 2, C], F32R)
        w_g_low = sb("w_g_low", [128, 2, C], F32R)
        w_v = sb("w_v", [128, 2, C + 1])
        g_bias = sb("g_bias", [128, 1])
        v_bias = sb("v_bias", [128, C + 1])
        a_row = sb("a_row", [128, C])
        pair_mask = sb("pair_mask", [128, 2])
        w_raw = sb("w_raw", [C, 4, C])
        w_fold = sb("w_fold", [C, 3, C])
        w_foldT = sb("w_foldT", [C, 3, 2, C])
        norm_col = sb("norm_col", [C, 4])
        norm_row = sb("norm_row", [128, 5, C])
        bias_col = sb("bias_col", [C, 3])
        bias_fold = sb("bias_fold", [C, 3])
        bias_wide = sb("bias_wide", [C, 2, 128])
        ab_col = sb("ab_col", [C, 2])
        b_row = sb("b_row", [128, C])
        col_tmp = sb("col_tmp", [C, 3])
        row_tmp = sb("row_tmp", [128, 3, C])

        xT_ps, g_ps, v_ps, probsT_ps, attn_ps = (psum(n) for n in ("xT_ps", "g_ps", "v_ps", "probsT_ps", "attn_ps"))
        score_ps = [psum(f"score_ps{i}") for i in range(2)]

        x_loaded = sem_ring("x_loaded")
        y_stored = sem_ring("y_stored")
        xT_made = sem_ring("xT_made")
        g_made = sem_ring("g_made")
        v_made = sem_ring("v_made")
        scores_made = sem_ring("scores_made")
        probsT_made = sem_ring("probsT_made")
        attn_made = sem_ring("attn_made")
        xT_kept = sem_ring("xT_kept")
        xT_rounded = sem_ring("xT_rounded")
        xT_split = sem_ring("xT_split")
        diag0_high = sem_ring("diag0_high")
        diag1_high = sem_ring("diag1_high")
        diag_low = sem_ring("diag_low")
        max_found = sem_ring("max_found")
        top_found = sem_ring("top_found")
        neg_top_found = sem_ring("neg_top_found")
        sum_inverted = sem_ring("sum_inverted")
        attn_kept = sem_ring("attn_kept")
        g_rounded = sem_ring("g_rounded")
        g_split = sem_ring("g_split")
        v_kept = sem_ring("v_kept")
        probs_found = sem_ring("probs_found")
        probsT_kept = sem_ring("probsT_kept")
        x_scaled = sem_ring("x_scaled")
        y_found = sem_ring("y_found")
        params_loaded = sem("params_loaded")
        pool_const = sem("pool_const")
        dve_setup = sem("dve_setup")
        pe_setup = sem("pe_setup")
        act_setup = sem("act_setup")

        COL_VAR, ROW_VAR, FOLDED, TRANSPOSED, BIASED, WIDE, DVE_READY = 1, 2, 23, 24, 25, 26, 37
        PARAM_DMAS = 4 + 4 + 5 + 3

        class Turn:

            def __init__(self, eng, r, dma):
                self.r = r
                self.uses = {k: eng.snap(r + k) if k else r for k in range(-1, 3)}
                self.dma = {k: eng.snap((r + k) * DMA_INC) for k in range(-1, 3)} if dma else {}

        def uses(r, n):
            k = n // RING + 1
            return r + k if isinstance(r, int) else r.uses[k]

        def dma_uses(r, n):
            k = n // RING + 1
            return DMA_INC * (r + k) if isinstance(r, int) else r.dma[k]

        def group(r, n):
            return (r if isinstance(r, int) else r.r) * RING + n

        def parts(n):
            return n % RING

        block = ctx.enter_context(nc.Block())

        def pipeline(eng, step, dma=False):
            for t in range(-3, 2 * RING):
                step(0, t, True)
            with eng.Fori(2, N // RING - 1) as r:
                turn = Turn(eng, r, dma)
                for t in range(RING):
                    step(turn, t, False)
            for t in range(RING + 3):
                step(N // RING - 1, t, True)

        def exists(r, n, peeled):
            return not peeled or 0 <= group(r, n) < N

        @block.sync
        def _(sp):
            for i, w in enumerate((wq, wk, wv, wo)):
                sp.dma_start(w_raw[:, i, :], w).then_inc(params_loaded, DMA_INC)
            for i, v in enumerate((gamma, beta, mean, var)):
                sp.dma_start(norm_col[:, i:i + 1], v.rearrange("(c o) -> c o", o=1)).then_inc(params_loaded, DMA_INC)
            for i, v in enumerate((gamma, beta, mean, var, bo)):
                sp.dma_start(norm_row[:, i, :], v.rearrange("(o c) -> o c", o=1).broadcast_to([128, C])).then_inc(params_loaded, DMA_INC)
            for i, v in enumerate((bq, bk, bv)):
                sp.dma_start(bias_col[:, i:i + 1], v.rearrange("(c o) -> c o", o=1)).then_inc(params_loaded, DMA_INC)

            def load(r, n, peeled):
                if not exists(r, n, peeled):
                    return
                if exists(r, n - RING, peeled):
                    sp.wait_ge(xT_made[parts(n)], uses(r, n - RING))
                    sp.wait_ge(x_scaled[parts(n)], uses(r, n - RING))
                sp.dma_start(x_in[:, parts(n), :, :], x_groups[group(r, n)]).then_inc(x_loaded[parts(n)], DMA_INC)

            def store(r, n, peeled):
                if not exists(r, n, peeled):
                    return
                sp.wait_ge(y_found[parts(n)], uses(r, n))
                sp.dma_start(out_groups[group(r, n)], y[:, parts(n), :, :]).then_inc(y_stored[parts(n)], DMA_INC)

            for n in range(2):
                load(0, n, True)

            def step(r, t, peeled):
                store(r, t - 3, peeled)
                load(r, t + RING + 1, peeled)

            for t in range(-3, 2 * RING):
                step(0, t, True)
            with sp.Fori(2, N // RING - 2) as r:
                turn = Turn(sp, r, False)
                for t in range(RING):
                    step(turn, t, False)
            for t in range(RING):
                step(N // RING - 2, t, True)
            for t in range(RING + 3):
                step(N // RING - 1, t, True)
            for s in y_stored:
                sp.wait_ge(s, DMA_INC * (N // RING))

        @block.gpsimd
        def _(pool):
            nc.gpsimd.memset(ident[:], 0.0).then_inc(pool_const, 1)
            nc.gpsimd.memset(w_g[:], 0.0).then_inc(pool_const, 1)
            nc.gpsimd.memset(w_v[:], 0.0).then_inc(pool_const, 1)
            nc.gpsimd.memset(v_aug[:], 1.0).then_inc(pool_const, 1)
            nc.gpsimd.memset(x_diag[:].bitcast(F32), 0.0).then_inc(pool_const, 1)
            nc.gpsimd.memset(pair_mask[:], 0.0).then_inc(pool_const, 1)
            pool.wait_ge(pool_const, 6)
            nc.gpsimd.affine_select(out=ident[:], in_=ident[:], compare_op=ALU.not_equal, fill=1.0, base=0,
                                    pattern=[[-1, 128]], channel_multiplier=1).then_inc(pool_const, 1)

            for h in range(2):
                pool.wait_ge(pool_const, 7 + h)
                nc.gpsimd.memset(pair_mask[h * C:(h + 1) * C, h:h + 1], 1.0).then_inc(pool_const, 1)

            a_b = a_row[:, None, :].broadcast_to([128, GROUP, C])
            mask_b = pair_mask[:, None, :, None].broadcast_to([128, PAIRS, 2, W])
            pool.wait_ge(dve_setup, DVE_READY)

            def step(r, t, peeled):
                n = t + 1
                if exists(r, n, peeled):
                    s = parts(n)
                    pool.wait_ge(xT_split[s], uses(r, n))
                    if exists(r, n - 2, peeled):
                        pool.wait_ge(scores_made[parts(n - 2)], uses(r, n - 2))
                    nc.gpsimd.tensor_tensor(x_diag[:, n % 2, 1], xT_low[:, n % 2, :, None, :].broadcast_to([128, PAIRS, 2, W]),
                                            mask_b, ALU.mult).then_inc(diag_low[s], 1)
                    pool.wait_ge(x_loaded[s], dma_uses(r, n))
                    if exists(r, n - RING, peeled):
                        pool.wait_ge(y_found[s], uses(r, n - RING))
                    nc.gpsimd.tensor_tensor(x_scaled_rows[:, s], x_in[:, s], a_b, ALU.mult).then_inc(x_scaled[s], 1)
                n = t + 2
                if exists(r, n, peeled):
                    s = parts(n)
                    pool.wait_ge(xT_rounded[s], uses(r, n))
                    nc.gpsimd.tensor_tensor(xT_low[:, n % 2], xT[:, n % 2], xT_high[:, n % 2],
                                            ALU.subtract).then_inc(xT_split[s], 1)

            pipeline(pool, step, dma=True)

        @block.scalar
        def _(act):
            act.wait_ge(dve_setup, ROW_VAR)
            nc.scalar.activation(col_tmp[:, 1:2], col_tmp[:, 0:1], ACT.Sqrt).then_inc(act_setup, 1)
            nc.scalar.activation(row_tmp[:, 1, :], row_tmp[:, 0, :], ACT.Sqrt).then_inc(act_setup, 1)

            def step(r, t, peeled):
                n = t + 2
                if exists(r, n, peeled):
                    s = parts(n)
                    act.wait_ge(xT_made[s], uses(r, n))
                    if exists(r, n - 2, peeled):
                        act.wait_ge(v_made[parts(n - 2)], uses(r, n - 2))
                        act.wait_ge(diag_low[parts(n - 2)], uses(r, n - 2))
                    nc.scalar.activation(xT[:, n % 2], xT_ps[:, 0:PAIRS * W].rearrange("p (k w) -> p k w", k=PAIRS),
                                         ACT.Copy).then_inc(xT_kept[s], 1)
                n = t + 1
                if exists(r, n, peeled):
                    s = parts(n)
                    act.wait_ge(xT_rounded[s], uses(r, n))
                    if exists(r, n - 2, peeled):
                        act.wait_ge(scores_made[parts(n - 2)], uses(r, n - 2))
                    nc.scalar.activation(x_diag[0:C, n % 2, 0, :, 0, :], xT_high[0:C, n % 2], ACT.Copy).then_inc(diag0_high[s], 1)
                n = t - 1
                if exists(r, n, peeled):
                    s = parts(n)
                    act.wait_ge(probsT_made[s], uses(r, n))
                    nc.scalar.activation(probsT[:, n % 2], probsT_ps[:].rearrange("p (s w) -> p s w", s=GROUP), ACT.Copy).then_inc(probsT_kept[s], 1)
                n = t + 1
                if exists(r, n, peeled):
                    s = parts(n)
                    act.wait_ge(g_made[s], uses(r, n))
                    nc.scalar.activation(g_high[:].rearrange("p k w -> p (k w)"), g_ps[:, 0:PAIRS * W], ACT.Identity,
                                         bias=g_bias[:, 0:1]).then_inc(g_rounded[s], 1)
                n = t
                if exists(r, n, peeled):
                    s = parts(n)
                    act.wait_ge(neg_top_found[s], uses(r, n))
                    for q in range(GROUP):
                        last = nc.scalar.activation(probs[:, q, :], score_ps[n % 2][:, q * W:(q + 1) * W], ACT.Exp,
                                                    bias=neg_top[:, s, q:q + 1])
                    last.then_inc(probs_found[s], 1)

            act.wait_ge(dve_setup, DVE_READY)
            pipeline(act, step)

        @block.vector
        def _(dve):
            done = [0]

            def chain(ins):
                done[0] += 1
                ins.then_inc(dve_setup, 1)
                dve.wait_ge(dve_setup, done[0])

            dve.wait_ge(params_loaded, DMA_INC * PARAM_DMAS)
            chain(nc.vector.tensor_scalar(col_tmp[:, 0:1], norm_col[:, 3:4], BN_EPS, None, ALU.add))
            chain(nc.vector.tensor_scalar(row_tmp[:, 0, :], norm_row[:, 3, :], BN_EPS, None, ALU.add))
            assert done[0] == ROW_VAR
            dve.wait_ge(act_setup, 2)

            def refine(root, v, tmp):
                chain(nc.vector.tensor_tensor(tmp, root, root, ALU.mult))
                chain(nc.vector.tensor_tensor(tmp, tmp, v, ALU.mult))
                chain(nc.vector.tensor_scalar(tmp, tmp, -0.5, 1.5, ALU.mult, ALU.add))
                chain(nc.vector.tensor_tensor(root, root, tmp, ALU.mult))

            chain(nc.vector.reciprocal(col_tmp[:, 2:3], col_tmp[:, 1:2]))
            refine(col_tmp[:, 2:3], col_tmp[:, 0:1], col_tmp[:, 1:2])
            chain(nc.vector.tensor_tensor(ab_col[:, 0:1], col_tmp[:, 2:3], norm_col[:, 0:1], ALU.mult))
            chain(nc.vector.tensor_tensor(ab_col[:, 1:2], ab_col[:, 0:1], norm_col[:, 2:3], ALU.mult))
            chain(nc.vector.tensor_tensor(ab_col[:, 1:2], norm_col[:, 1:2], ab_col[:, 1:2], ALU.subtract))
            chain(nc.vector.reciprocal(row_tmp[:, 2, :], row_tmp[:, 1, :]))
            refine(row_tmp[:, 2, :], row_tmp[:, 0, :], row_tmp[:, 1, :])
            chain(nc.vector.tensor_tensor(a_row[:], row_tmp[:, 2, :], norm_row[:, 0, :], ALU.mult))
            chain(nc.vector.tensor_tensor(b_row[:], a_row[:], norm_row[:, 2, :], ALU.mult))
            chain(nc.vector.tensor_tensor(b_row[:], norm_row[:, 1, :], b_row[:], ALU.subtract))
            chain(nc.vector.tensor_tensor(b_row[:], b_row[:], norm_row[:, 4, :], ALU.add))
            chain(nc.vector.tensor_scalar(w_fold[:, 0, :], w_raw[:, 0, :], ab_col[:, 0:1], SCALE, ALU.mult, ALU.mult))
            chain(nc.vector.tensor_scalar(w_fold[:, 1, :], w_raw[:, 1, :], ab_col[:, 0:1], None, ALU.mult))
            chain(nc.vector.tensor_scalar(w_fold[:, 2, :], w_raw[:, 2, :], ab_col[:, 0:1], None, ALU.mult))
            dve.wait_ge(pe_setup, 1)
            chain(nc.vector.tensor_tensor(bias_fold[:], attn_ps[0:C, 0:3], bias_col[:], ALU.add))
            assert done[0] == FOLDED
            dve.wait_ge(pe_setup, 2)
            chain(nc.vector.tensor_copy(w_foldT[:], g_ps[0:C, 0:3 * 2 * C].rearrange("p (k h c) -> p k h c", k=3, h=2)))
            assert done[0] == TRANSPOSED
            chain(nc.vector.tensor_scalar(bias_fold[:, 0:1], bias_fold[:, 0:1], SCALE, None, ALU.mult))
            assert done[0] == BIASED
            chain(nc.vector.tensor_copy(bias_wide[:], bias_fold[:, 0:3:2, None].broadcast_to([C, 2, 128])))
            assert done[0] == WIDE
            dve.wait_ge(pe_setup, 3)
            dve.wait_ge(pool_const, 9)
            for h in range(2):
                p = slice(h * C, (h + 1) * C)
                chain(nc.vector.tensor_copy(w_g[p, h, :], v_ps[p, 0:C]))
                chain(nc.vector.tensor_copy(w_v[p, h, 1:C + 1], v_ps[p, C:2 * C]))
                chain(nc.vector.tensor_copy(w_v[p, h, 0:1], v_ps[p, 2 * C + 1:2 * C + 2]))
            chain(nc.vector.tensor_copy(w_g_high[:], w_g[:]))
            chain(nc.vector.tensor_tensor(w_g_low[:], w_g[:], w_g_high[:], ALU.subtract))
            chain(nc.vector.tensor_copy(g_bias[:], v_ps[:, 2 * C:2 * C + 1]))
            chain(nc.vector.tensor_copy(v_bias[:, 0:1], v_ps[:, 2 * C + 2:2 * C + 3]))
            chain(nc.vector.tensor_tensor(v_bias[:, 1:C + 1], v_ps[:, 3 * C:4 * C], b_row[:], ALU.add))
            assert done[0] == DVE_READY, done[0]

            v_bias_b = v_bias[:, None, :].broadcast_to([128, GROUP, C + 1])

            def step(r, t, peeled):
                n = t
                if exists(r, n, peeled):
                    s = parts(n)
                    dve.wait_ge(v_made[s], uses(r, n))
                    nc.vector.tensor_tensor(v_aug[:, s, :, 0:C + 1], v_ps[:, 0:GROUP * (C + 1)].rearrange("p (s c) -> p s c", s=GROUP),
                                            v_bias_b, ALU.add).then_inc(v_kept[s], 1)
                n = t - 3
                if exists(r, n, peeled):
                    s = parts(n)
                    dve.wait_ge(attn_made[s], uses(r, n))
                    nc.vector.reciprocal(inv_sum[:, s, :], attn_ps[:, 0:GROUP * (C + 1)].rearrange("p (s c) -> p s c", s=GROUP)[:, :, C]) \
                        .then_inc(sum_inverted[s], 1)
                n = t - 3
                if exists(r, n, peeled):
                    s = parts(n)
                    dve.wait_ge(sum_inverted[s], uses(r, n))
                    nc.vector.tensor_tensor(attn[:], attn_ps[:, 0:GROUP * (C + 1)].rearrange("p (s c) -> p s c", s=GROUP)[:, :, 0:C],
                                            inv_sum[:, s, :, None].broadcast_to([128, GROUP, C]),
                                            ALU.mult).then_inc(attn_kept[s], 1)
                n = t
                if exists(r, n, peeled):
                    s = parts(n)
                    dve.wait_ge(scores_made[s], uses(r, n))
                    nc.vector.tensor_reduce(row_max[:, s, :], score_ps[n % 2][:].rearrange("p (s w) -> p s w", s=GROUP),
                                            AX_X, ALU.max).then_inc(max_found[s], 1)
                n = t + 1
                if exists(r, n, peeled):
                    s = parts(n)
                    dve.wait_ge(xT_rounded[s], uses(r, n))
                    if exists(r, n - 2, peeled):
                        dve.wait_ge(scores_made[parts(n - 2)], uses(r, n - 2))
                    nc.vector.tensor_copy(x_diag[C:2 * C, n % 2, 0, :, 1, :], xT_high[C:2 * C, n % 2]).then_inc(diag1_high[s], 1)
                n = t
                if exists(r, n, peeled):
                    s = parts(n)
                    dve.wait_ge(max_found[s], uses(r, n))
                    dve.wait_ge(v_kept[s], uses(r, n))
                    nc.vector.tensor_tensor(top[:, s, :], v_aug[:, s, :, 0], row_max[:, s, :], ALU.add).then_inc(top_found[s], 1)
                n = t + 2
                if exists(r, n, peeled):
                    s = parts(n)
                    dve.wait_ge(xT_kept[s], uses(r, n))
                    nc.vector.tensor_copy(xT_high[:, n % 2], xT[:, n % 2]).then_inc(xT_rounded[s], 1)
                n = t
                if exists(r, n, peeled):
                    s = parts(n)
                    dve.wait_ge(top_found[s], uses(r, n))
                    nc.vector.tensor_tensor(neg_top[:, s, :], v_aug[:, s, :, 0], top[:, s, :], ALU.subtract).then_inc(neg_top_found[s], 1)
                n = t - 3
                if exists(r, n, peeled):
                    s = parts(n)
                    dve.wait_ge(attn_kept[s], uses(r, n))
                    dve.wait_ge(x_scaled[s], uses(r, n))
                    if exists(r, n - RING, peeled):
                        dve.wait_ge(y_stored[s], dma_uses(r, n - RING))
                    nc.vector.tensor_tensor(y[:, s], attn[:], x_scaled_rows[:, s], ALU.add).then_inc(y_found[s], 1)
                n = t + 1
                if exists(r, n, peeled):
                    s = parts(n)
                    dve.wait_ge(g_rounded[s], uses(r, n))
                    nc.vector.scalar_tensor_tensor(out=g_low[:].rearrange("p k w -> p (k w)"), in0=g_ps[:, 0:PAIRS * W],
                                                   scalar=g_bias[:, 0:1], in1=g_high[:].rearrange("p k w -> p (k w)"),
                                                   op0=ALU.add, op1=ALU.subtract).then_inc(g_split[s], 1)

            pipeline(dve, step, dma=True)

        @block.tensor
        def _(pe):
            pe.wait_ge(dve_setup, FOLDED - 1)
            for i in range(3):
                last = nc.tensor.matmul(attn_ps[0:C, i:i + 1], w_raw[:, i, :], ab_col[:, 1:2], start=True, stop=True)
            last.then_inc(pe_setup, 1)
            pe.wait_ge(pool_const, 7)
            for i in range(3):
                for h in range(2):
                    last = nc.tensor.transpose(g_ps[0:C, (2 * i + h) * C:(2 * i + h + 1) * C], w_fold[:, i, :],
                                               ident[0:C, 0:C])
            last.then_inc(pe_setup, 1)
            pe.wait_ge(dve_setup, WIDE)
            wqT, wkT, wvT = (w_foldT[:, i].rearrange("p h c -> p (h c)") for i in range(3))
            for o, lhsT, rhs in ((0, wqT, w_foldT[:, 1, 0, :]),
                                 (C, wvT, w_raw[:, 3, :]),
                                 (2 * C, wkT, bias_fold[:, 0:1]),
                                 (2 * C + 1, wqT, bias_fold[:, 1:2]),
                                 (2 * C + 2, bias_wide[:, 0, :], bias_fold[:, 1:2]),
                                 (3 * C, bias_wide[:, 1, :], w_raw[:, 3, :])):
                last = nc.tensor.matmul(v_ps[:, o:o + rhs.shape[1]], lhsT, rhs, start=True, stop=True)
            last.then_inc(pe_setup, 1)
            pe.wait_ge(dve_setup, DVE_READY)

            w_g_high_all = w_g_high[:].rearrange("p h c -> p (h c)")
            w_g_low_all = w_g_low[:].rearrange("p h c -> p (h c)")
            w_v_all = w_v[:].rearrange("p h c -> p (h c)")

            def step(r, t, peeled):
                n = t
                if exists(r, n, peeled):
                    s = parts(n)
                    pe.wait_ge(g_rounded[s], uses(r, n))
                    pe.wait_ge(diag0_high[s], uses(r, n))
                    pe.wait_ge(diag1_high[s], uses(r, n))
                    pe.wait_ge(diag_low[s], uses(r, n))
                    score_parts = ((g_high, 1), (g_high, 0), (g_low, 0))
                    for k in range(PAIRS):
                        for i, (g_part, x_part) in enumerate(score_parts):
                            if g_part is g_low and k == 0:
                                pe.wait_ge(g_split[s], uses(r, n))
                            last = nc.tensor.matmul(score_ps[n % 2][:, k * 2 * W:(k + 1) * 2 * W], g_part[:, k, :],
                                                    x_diag[:, n % 2, x_part, k].rearrange("p h w -> p (h w)"),
                                                    start=(i == 0), stop=(i == len(score_parts) - 1))
                    last.then_inc(scores_made[s], 1)
                n = t - 1
                if exists(r, n, peeled):
                    s = parts(n)
                    pe.wait_ge(probs_found[s], uses(r, n))
                    if exists(r, n - 1, peeled):
                        pe.wait_ge(probsT_kept[parts(n - 1)], uses(r, n - 1))
                    for q in range(GROUP):
                        last = nc.tensor.transpose(probsT_ps[:, q * W:(q + 1) * W], probs[:, q, :], ident[:])
                    last.then_inc(probsT_made[s], 1)
                n = t + 3
                if exists(r, n, peeled):
                    s = parts(n)
                    pe.wait_ge(x_loaded[s], dma_uses(r, n))
                    if exists(r, n - 1, peeled):
                        pe.wait_ge(xT_kept[parts(n - 1)], uses(r, n - 1))
                    for k in range(PAIRS):
                        last = nc.tensor.transpose(xT_ps[:, k * W:(k + 1) * W],
                                                   x_in[:, s, 2 * k:2 * k + 2, :].rearrange("p s c -> p (s c)"), ident[:])
                    last.then_inc(xT_made[s], 1)
                n = t + 1
                if exists(r, n, peeled):
                    s = parts(n)
                    pe.wait_ge(xT_split[s], uses(r, n))
                    g_parts = ((w_g_low_all, xT_high), (w_g_high_all, xT_low), (w_g_high_all, xT_high))
                    for i, (w_part, x_part) in enumerate(g_parts):
                        last = nc.tensor.matmul(g_ps[:, 0:PAIRS * W], w_part, x_part[:, n % 2].rearrange("p k w -> p (k w)"),
                                                start=(i == 0), stop=(i == len(g_parts) - 1))
                    last.then_inc(g_made[s], 1)
                    pe.wait_ge(xT_kept[s], uses(r, n))
                    if exists(r, n - 1, peeled):
                        pe.wait_ge(v_kept[parts(n - 1)], uses(r, n - 1))
                    for k in range(PAIRS):
                        last = nc.tensor.matmul(v_ps[:, k * 2 * (C + 1):(k + 1) * 2 * (C + 1)], xT[:, n % 2, k, :], w_v_all,
                                                start=True, stop=True)
                    last.then_inc(v_made[s], 1)
                n = t - 2
                if exists(r, n, peeled):
                    s = parts(n)
                    pe.wait_ge(probsT_kept[s], uses(r, n))
                    if exists(r, n - 1, peeled):
                        pe.wait_ge(attn_kept[parts(n - 1)], uses(r, n - 1))
                    for q in range(GROUP):
                        last = nc.tensor.matmul(attn_ps[:, q * (C + 1):(q + 1) * (C + 1)], probsT[:, n % 2, q, :],
                                                v_aug[:, s, q, 1:VW], start=True, stop=True)
                    last.then_inc(attn_made[s], 1)

            pipeline(pe, step, dma=True)


_PARAMS = ["gamma", "beta", "moving_mean", "moving_var", "Wq", "bq", "Wk", "bk", "Wv", "bv", "Wo", "bo"]


def kernel(**inputs):
    import numpy as np
    import concourse.bacc as bacc
    from concourse.bass_utils import run_bass_kernel_spmd

    nc = bacc.Bacc("TRN2", target_bir_lowering=False, num_devices=1)
    arrays, aps = {}, []
    for name in ["x"] + ["L0_conv_" + p for p in _PARAMS]:
        a = np.ascontiguousarray(inputs[name])
        arrays[f"in_{name}"] = a
        aps.append(nc.dram_tensor(f"in_{name}", a.shape, mybir.dt.from_np(a.dtype), kind="ExternalInput").ap())
    aps.append(nc.dram_tensor("out_0", inputs["x"].shape, F32, kind="ExternalOutput").ap())
    build(nc, *aps)
    r = run_bass_kernel_spmd(nc, [arrays], core_ids=[0])
    return r.results[0]["out_0"]
```
